# Optimizing a Trainium2 kernel written in Bass

```python
import numpy as np
import jax
import jax.numpy as jnp

def _softmax(x, axis=-1):
    return jax.nn.softmax(x, axis=axis)

def _gelu(x):
    return jax.nn.gelu(x, approximate=True)

def _silu(x):
    return jax.nn.silu(x)

def _sigmoid(x):
    return jax.nn.sigmoid(x)

def _layernorm(x, axis=-1, eps=1e-05):
    m = jnp.mean(x, axis=axis, keepdims=True)
    v = jnp.var(x, axis=axis, keepdims=True)
    return (x - m) / jnp.sqrt(v + eps)

def _scatter_add(tgt, idx, src, axis=0):
    return tgt.at[idx].add(src)

def _segment_sum(src, seg, n):
    return jax.ops.segment_sum(src, seg, n)
kernel_name = 'mk_flamingo_gated_d1_seqx_r2_91b380'

def setup_inputs(seed: int=0):
    np.random.seed(seed)
    _w = jnp.asarray

    def _rec_inputs():
        import jax
        import jax.numpy as jnp
        _rk = jax.random.key(seed)
        x = 4.136e-05 + 0.9999 * jax.random.normal(jax.random.fold_in(_rk, 1), (4, 1024, 1024), jnp.float32)
        _lenS = 1024 - jax.random.randint(jax.random.fold_in(_rk, 7), (4,), 0, max(1, 1024 // 4) + 1, jnp.int32)
        _lenS2 = 1024 - jax.random.randint(jax.random.fold_in(_rk, 8), (4,), 0, max(1, 1024 // 4) + 1, jnp.int32)
        _ctx_1024P = jax.random.normal(jax.random.fold_in(_rk, 11), (4, 16, 512), jnp.float32)
        _ctx_1024c = jax.random.dirichlet(jax.random.fold_in(_rk, 511), 0.3 * jnp.ones((16,), jnp.float32), (4, 1024))
        _ctx_1024t = jnp.einsum('bsk,bkd->bsd', _ctx_1024c, _ctx_1024P)
        _ctx_1024t = _ctx_1024t * jax.lax.rsqrt(jnp.mean(jnp.square(_ctx_1024t)) + 1e-12) * 0.953939
        ctx_1024 = -0.000292821 + 1.00034 * (_ctx_1024t + 0.3 * jax.random.normal(jax.random.fold_in(_rk, 611), (4, 1024, 512), jnp.float32))
        _g = jax.random.normal(jax.random.fold_in(_rk, 9001), (2, 1), jnp.float32)
        _g = jnp.sign(_g) * jnp.maximum(jnp.abs(_g), 1.0) + (_g == 0) * 1.0
        g_xattn = _g[0]
        g_ffn = _g[1]
        return (x, ctx_1024, g_xattn, g_ffn)
    x, ctx_1024, g_xattn, g_ffn = _rec_inputs()

    def _L0_xattn_setup():
        import jax, jax.numpy as jnp
        import numpy as np
        import math
        B, L, DM = (2, 1024, 512)
        DS, DC, EXP = (16, 4, 2)
        DI = EXP * DM
        DR = math.ceil(DM / 16)
        DT_MIN, DT_MAX, DT_FLOOR = (0.001, 0.1, 0.0001)

        def _ssm_forward(hidden_states, z, in_proj_w, conv_w, conv_b, x_proj_w, dt_proj_w, dt_proj_b, A_log, D):
            b = hidden_states.shape[0]
            x = jnp.einsum('ed,bld->bel', in_proj_w, hidden_states)
            xp = jnp.pad(x, ((0, 0), (0, 0), (DC - 1, 0)))
            xc = jax.lax.conv_general_dilated(xp, conv_w[:, None, :], window_strides=(1,), padding='VALID', dimension_numbers=('NCH', 'OIH', 'NCH'), feature_group_count=DI)
            u = jax.nn.silu(xc + conv_b[None, :, None])
            x_dbl = jnp.einsum('ke,bel->bkl', x_proj_w, u)
            dt_lo = x_dbl[:, :DR]
            Bm = x_dbl[:, DR:DR + DS]
            Cm = x_dbl[:, DR + DS:]
            delta = jax.nn.softplus(jnp.einsum('er,brl->bel', dt_proj_w, dt_lo) + dt_proj_b[None, :, None])
            A = -jnp.exp(A_log)

            def step(state, xs):
                d_t, B_t, C_t, u_t = xs
                dA = jnp.exp(d_t[..., None] * A)
                state = state * dA + (d_t * u_t)[..., None] * B_t[:, None, :]
                y_t = jnp.einsum('ben,bn->be', state, C_t)
                return (state, y_t)
            xs = (jnp.moveaxis(delta, -1, 0), jnp.moveaxis(Bm, -1, 0), jnp.moveaxis(Cm, -1, 0), jnp.moveaxis(u, -1, 0))
            state0 = jnp.zeros((b, DI, DS), delta.dtype)
            _, ys = jax.lax.scan(step, state0, xs)
            y = jnp.moveaxis(ys, 0, -1)
            y = y + D[None, :, None] * u
            y = y * jax.nn.silu(z)
            return jnp.swapaxes(y, 1, 2)
        key = jax.random.key(seed)
        ks = jax.random.split(key, 8)
        hidden_states = jax.random.normal(ks[0], (B, L, DM), jnp.float32)
        z = jax.random.normal(ks[1], (B, DI, L), jnp.float32)
        in_proj_w = jax.random.normal(ks[2], (DI, DM), jnp.float32) * DM ** (-0.5)
        conv_w = jax.random.normal(ks[3], (DI, DC), jnp.float32) * DC ** (-0.5)
        conv_b = jnp.zeros((DI,), jnp.float32)
        x_proj_w = jax.random.normal(ks[4], (DR + 2 * DS, DI), jnp.float32) * DI ** (-0.5)
        dt_std = DR ** (-0.5)
        dt_proj_w = jax.random.uniform(ks[5], (DI, DR), jnp.float32, -dt_std, dt_std)
        dt = jnp.exp(jax.random.uniform(ks[6], (DI,), jnp.float32) * (math.log(DT_MAX) - math.log(DT_MIN)) + math.log(DT_MIN))
        dt = jnp.clip(dt, DT_FLOOR)
        dt_proj_b = dt + jnp.log(-jnp.expm1(-dt))
        A_log = jnp.log(jnp.broadcast_to(jnp.arange(1, DS + 1, dtype=jnp.float32), (DI, DS)))
        D = jnp.ones((DI,), jnp.float32)
        return dict(hidden_states=hidden_states, z=z, in_proj_w=in_proj_w, conv_w=conv_w, conv_b=conv_b, x_proj_w=x_proj_w, dt_proj_w=dt_proj_w, dt_proj_b=dt_proj_b, A_log=A_log, D=D)
    _L0_xattn_all = _L0_xattn_setup()
    _L0_xattn_in = {k: v for k, v in _L0_xattn_all.items() if k in ('in_proj_w', 'conv_w', 'conv_b', 'x_proj_w', 'dt_proj_w', 'dt_proj_b', 'A_log', 'D')}
    del _L0_xattn_all

    def _L0_ffn_setup():
        import jax, jax.numpy as jnp
        import numpy as np
        CAPACITY = 0.125
        HEAD_DIM = 128
        N_HEADS = 16
        N_KV_HEADS = 8
        ROPE_THETA = 10000.0
        EPS = 1e-06

        def _rms_norm(x, w):
            return x * jax.lax.rsqrt(jnp.mean(x * x, axis=-1, keepdims=True) + EPS) * w

        def _rotate_half(t):
            h = t.shape[-1] // 2
            return jnp.concatenate([-t[..., h:], t[..., :h]], axis=-1)
        key = jax.random.key(seed)
        ks = jax.random.split(key, 12)
        B, T, D = (4, 2048, 1024)
        I = 4096
        s = 0.02
        return {'hidden_states': jax.random.normal(ks[0], (B, T, D), jnp.float32), 'w_router': jax.random.normal(ks[1], (D,), jnp.float32) * s, 'wq': jax.random.normal(ks[2], (D, N_HEADS * HEAD_DIM), jnp.float32) * s, 'bq': jnp.zeros((N_HEADS * HEAD_DIM,), jnp.float32), 'wk': jax.random.normal(ks[3], (D, N_KV_HEADS * HEAD_DIM), jnp.float32) * s, 'bk': jnp.zeros((N_KV_HEADS * HEAD_DIM,), jnp.float32), 'wv': jax.random.normal(ks[4], (D, N_KV_HEADS * HEAD_DIM), jnp.float32) * s, 'bv': jnp.zeros((N_KV_HEADS * HEAD_DIM,), jnp.float32), 'wo': jax.random.normal(ks[5], (N_HEADS * HEAD_DIM, D), jnp.float32) * s, 'w_gate': jax.random.normal(ks[6], (D, I), jnp.float32) * s, 'w_up': jax.random.normal(ks[7], (D, I), jnp.float32) * s, 'w_down': jax.random.normal(ks[8], (I, D), jnp.float32) * s, 'ln1_w': jnp.ones((D,), jnp.float32), 'ln2_w': jnp.ones((D,), jnp.float32)}
    _L0_ffn_all = _L0_ffn_setup()
    _L0_ffn_in = {k: v for k, v in _L0_ffn_all.items() if k in ('w_router', 'wq', 'bq', 'wk', 'bk', 'wv', 'bv', 'wo', 'w_gate', 'w_up', 'w_down', 'ln1_w', 'ln2_w')}
    del _L0_ffn_all
    return {'x': x, 'ctx_1024': ctx_1024, 'g_xattn': g_xattn, 'g_ffn': g_ffn, 'L0_xattn_in_proj_w': _L0_xattn_in['in_proj_w'], 'L0_xattn_conv_w': _L0_xattn_in['conv_w'], 'L0_xattn_conv_b': _L0_xattn_in['conv_b'], 'L0_xattn_x_proj_w': _L0_xattn_in['x_proj_w'], 'L0_xattn_dt_proj_w': _L0_xattn_in['dt_proj_w'], 'L0_xattn_dt_proj_b': _L0_xattn_in['dt_proj_b'], 'L0_xattn_A_log': _L0_xattn_in['A_log'], 'L0_xattn_D': _L0_xattn_in['D'], 'L0_ffn_w_router': _L0_ffn_in['w_router'], 'L0_ffn_wq': _L0_ffn_in['wq'], 'L0_ffn_bq': _L0_ffn_in['bq'], 'L0_ffn_wk': _L0_ffn_in['wk'], 'L0_ffn_bk': _L0_ffn_in['bk'], 'L0_ffn_wv': _L0_ffn_in['wv'], 'L0_ffn_bv': _L0_ffn_in['bv'], 'L0_ffn_wo': _L0_ffn_in['wo'], 'L0_ffn_w_gate': _L0_ffn_in['w_gate'], 'L0_ffn_w_up': _L0_ffn_in['w_up'], 'L0_ffn_w_down': _L0_ffn_in['w_down'], 'L0_ffn_ln1_w': _L0_ffn_in['ln1_w'], 'L0_ffn_ln2_w': _L0_ffn_in['ln2_w']}

def reference(x, ctx_1024, g_xattn, g_ffn, L0_xattn_in_proj_w, L0_xattn_conv_w, L0_xattn_conv_b, L0_xattn_x_proj_w, L0_xattn_dt_proj_w, L0_xattn_dt_proj_b, L0_xattn_A_log, L0_xattn_D, L0_ffn_w_router, L0_ffn_wq, L0_ffn_bq, L0_ffn_wk, L0_ffn_bk, L0_ffn_wv, L0_ffn_bv, L0_ffn_wo, L0_ffn_w_gate, L0_ffn_w_up, L0_ffn_w_down, L0_ffn_ln1_w, L0_ffn_ln2_w):
    import jax
    import jax.numpy as jnp

    def _L0_xattn_ref(hidden_states, z, in_proj_w, conv_w, conv_b, x_proj_w, dt_proj_w, dt_proj_b, A_log, D):
        import jax, jax.numpy as jnp
        import numpy as np
        import math
        B, L, DM = (2, 1024, 512)
        DS, DC, EXP = (16, 4, 2)
        DI = EXP * DM
        DR = math.ceil(DM / 16)
        DT_MIN, DT_MAX, DT_FLOOR = (0.001, 0.1, 0.0001)

        def _ssm_forward(hidden_states, z, in_proj_w, conv_w, conv_b, x_proj_w, dt_proj_w, dt_proj_b, A_log, D):
            b = hidden_states.shape[0]
            x = jnp.einsum('ed,bld->bel', in_proj_w, hidden_states)
            xp = jnp.pad(x, ((0, 0), (0, 0), (DC - 1, 0)))
            xc = jax.lax.conv_general_dilated(xp, conv_w[:, None, :], window_strides=(1,), padding='VALID', dimension_numbers=('NCH', 'OIH', 'NCH'), feature_group_count=DI)
            u = jax.nn.silu(xc + conv_b[None, :, None])
            x_dbl = jnp.einsum('ke,bel->bkl', x_proj_w, u)
            dt_lo = x_dbl[:, :DR]
            Bm = x_dbl[:, DR:DR + DS]
            Cm = x_dbl[:, DR + DS:]
            delta = jax.nn.softplus(jnp.einsum('er,brl->bel', dt_proj_w, dt_lo) + dt_proj_b[None, :, None])
            A = -jnp.exp(A_log)

            def step(state, xs):
                d_t, B_t, C_t, u_t = xs
                dA = jnp.exp(d_t[..., None] * A)
                state = state * dA + (d_t * u_t)[..., None] * B_t[:, None, :]
                y_t = jnp.einsum('ben,bn->be', state, C_t)
                return (state, y_t)
            xs = (jnp.moveaxis(delta, -1, 0), jnp.moveaxis(Bm, -1, 0), jnp.moveaxis(Cm, -1, 0), jnp.moveaxis(u, -1, 0))
            state0 = jnp.zeros((b, DI, DS), delta.dtype)
            _, ys = jax.lax.scan(step, state0, xs)
            y = jnp.moveaxis(ys, 0, -1)
            y = y + D[None, :, None] * u
            y = y * jax.nn.silu(z)
            return jnp.swapaxes(y, 1, 2)
        return _ssm_forward(hidden_states, z, in_proj_w, conv_w, conv_b, x_proj_w, dt_proj_w, dt_proj_b, A_log, D)

    def _L0_ffn_ref(hidden_states, w_router, wq, bq, wk, bk, wv, bv, wo, w_gate, w_up, w_down, ln1_w, ln2_w):
        import jax, jax.numpy as jnp
        import numpy as np
        CAPACITY = 0.125
        HEAD_DIM = 128
        N_HEADS = 16
        N_KV_HEADS = 8
        ROPE_THETA = 10000.0
        EPS = 1e-06

        def _rms_norm(x, w):
            return x * jax.lax.rsqrt(jnp.mean(x * x, axis=-1, keepdims=True) + EPS) * w

        def _rotate_half(t):
            h = t.shape[-1] // 2
            return jnp.concatenate([-t[..., h:], t[..., :h]], axis=-1)
        B, T, D = hidden_states.shape
        k = max(1, int(T * CAPACITY))
        scores = jnp.einsum('btd,d->bt', hidden_states, w_router)
        _, idx = jax.lax.top_k(scores, k)
        idx = jnp.sort(idx, axis=-1)
        b = jnp.arange(B)[:, None]
        sel = hidden_states[b, idx]
        sel_scores = scores[b, idx]
        S = B * k
        x = sel.reshape(S, D)
        pos = idx.reshape(S)
        inv_freq = 1.0 / ROPE_THETA ** (jnp.arange(0, HEAD_DIM, 2, dtype=jnp.float32) / HEAD_DIM)
        ang = pos.astype(jnp.float32)[:, None] * inv_freq
        cos = jnp.concatenate([jnp.cos(ang), jnp.cos(ang)], axis=-1)[:, None, :]
        sin = jnp.concatenate([jnp.sin(ang), jnp.sin(ang)], axis=-1)[:, None, :]
        h = _rms_norm(x, ln1_w)
        q = (h @ wq + bq).reshape(S, N_HEADS, HEAD_DIM)
        kk = (h @ wk + bk).reshape(S, N_KV_HEADS, HEAD_DIM)
        v = (h @ wv + bv).reshape(S, N_KV_HEADS, HEAD_DIM)
        q = q * cos + _rotate_half(q) * sin
        kk = kk * cos + _rotate_half(kk) * sin
        rep = N_HEADS // N_KV_HEADS
        kk = jnp.repeat(kk, rep, axis=1)
        v = jnp.repeat(v, rep, axis=1)
        att = jnp.einsum('shd,thd->hst', q, kk) / np.sqrt(HEAD_DIM)
        causal = jnp.tril(jnp.ones((S, S), bool))
        att = jnp.where(causal[None], att, jnp.finfo(att.dtype).min)
        att = jax.nn.softmax(att, axis=-1)
        attn_out = jnp.einsum('hst,thd->shd', att, v).reshape(S, N_HEADS * HEAD_DIM) @ wo
        x1 = x + attn_out
        h2 = _rms_norm(x1, ln2_w)
        mlp = jax.nn.silu(h2 @ w_gate) * (h2 @ w_up) @ w_down
        processed = x1 + mlp
        gate = jax.nn.sigmoid(sel_scores).reshape(S, 1)
        gated = gate * processed + (1.0 - gate) * x
        output = hidden_states.at[b, idx].set(gated.reshape(B, k, D))
        return output
    x = x + jnp.tanh(g_xattn[0]) * _L0_xattn_ref(ctx_1024, _layernorm(x, axis=-1), L0_xattn_in_proj_w, L0_xattn_conv_w, L0_xattn_conv_b, L0_xattn_x_proj_w, L0_xattn_dt_proj_w, L0_xattn_dt_proj_b, L0_xattn_A_log, L0_xattn_D)
    x = x + jnp.tanh(g_ffn[0]) * _L0_ffn_ref(_layernorm(x, axis=-1), L0_ffn_w_router, L0_ffn_wq, L0_ffn_bq, L0_ffn_wk, L0_ffn_bk, L0_ffn_wv, L0_ffn_bv, L0_ffn_wo, L0_ffn_w_gate, L0_ffn_w_up, L0_ffn_w_down, L0_ffn_ln1_w, L0_ffn_ln2_w)
    return x

_drawn_inputs = setup_inputs


def setup_inputs(seed=0):
    import zlib

    import numpy as np

    out = dict(_drawn_inputs(seed))
    spreads = {'L0_xattn_conv_b': (0.0, 0.1),
     'L0_xattn_D': (1.0, 0.2),
     'L0_ffn_bq': (0.0, 0.8),
     'L0_ffn_bk': (0.0, 0.8),
     'L0_ffn_bv': (0.0, 0.1),
     'L0_ffn_ln1_w': (1.0, 0.2),
     'L0_ffn_ln2_w': (1.0, 0.2)}
    factors = {}
    for name, (base, spread) in spreads.items():
        noise = np.random.default_rng([zlib.crc32(name.encode()), seed]).standard_normal(out[name].shape)
        drawn = base * np.exp(spread * noise) if base else spread * noise
        out[name] = jnp.asarray(drawn.astype(out[name].dtype))
    for name, factor in factors.items():
        out[name] = (out[name] * factor).astype(out[name].dtype)
    return out
```

```python
import concourse.bass as bass
from concourse import mybir
from contextlib import ExitStack
import numpy as np

F32 = mybir.dt.float32
I32 = mybir.dt.int32
ALU = mybir.AluOpType
ACT = mybir.ActivationFunctionType
AXX = mybir.AxisListType.X

NB, L, DC, DI = 4, 1024, 512, 1024
P = 128
NE = DI // P
NK = DC // P
NS, NR, TAPS = 16, 32, 4
ND = NR + 2 * NS
STEPS = NB * NE
HALF = 512
H2 = L // HALF
LN_EPS = 1e-5
TOPK = 128
S = NB * TOPK
NH, NKV, DH = 16, 8, 128
NI = 4096 // P
RMS_EPS = 1e-6


class Chain:

    def __init__(self, eng, sem, base=0):
        self.eng, self.sem, self.base, self.n = eng, sem, base, 0

    def did(self, ins):
        ins.then_inc(self.sem, 1)
        self.n += 1

    def wait(self):
        self.eng.wait_ge(self.sem, self.base + self.n)


def halves(ap, h):
    return ap[:, h * HALF:(h + 1) * HALF]


def project_stage(nc, t, ctx):
    def sb(name, shape):
        return ctx.enter_context(nc.sbuf_tensor("p_" + name, shape, F32))

    def sem(name):
        return nc.alloc_semaphore("p_" + name)

    w_in = sb("w_in", [P, NK, DI])
    w_x = sb("w_x", [P, NE, ND])
    conv = sb("conv", [P, NE, TAPS + 1])
    ctxT = sb("ctxT", [P, NB * NK * L])
    raw = sb("raw", [P, 2, TAPS - 1 + L])
    ug = sb("ug", [P, 2, 2, L])
    xz = sb("xz", [P, 2, L])
    stats = sb("stats", [P, 2, H2 * 6])
    mv = sb("mv", [P, 2, 2])
    rstd = sb("rstd", [P, 2])
    shift = sb("shift", [P, 2])
    minus_half = sb("minus_half", [P, 1])
    carrier = sb("carrier", [P, 1])
    xd = sb("xd", [ND, L])
    ps = [ctx.enter_context(nc.psum_tensor(f"p_x{j}", [P, L], F32)) for j in range(2)]
    ps_d = ctx.enter_context(nc.psum_tensor("p_xdp", [P, L], F32))

    weights, ctx_in = sem("weights"), sem("ctx")
    x_in = [sem(f"x_in{j}") for j in range(2)]
    projected, raw_copied, first_tap, taps = sem("projected"), sem("raw_copied"), sem("first_tap"), sem("taps")
    pads, stat_chain, var_ready, rstd_ready, shift_ready = sem("pads"), sem("stat"), sem("var"), sem("rstd"), sem("shift_r")
    u_ready, gate_ready, xd_sums, xd_copied, xd_out = sem("u"), sem("gate"), sem("xd_sums"), sem("xd_copied"), sem("xd_out")
    ug_out = [sem(f"ug_out{j}") for j in range(2)]
    exponent = sem("exponent")

    with nc.Block() as block:
        @block.sync
        def _(sp):
            sp.dma_start(w_in[:], t["w_in"]).then_inc(weights, 16)
            sp.dma_start(conv[:], t["conv"]).then_inc(weights, 16)
            sp.dma_start(w_x[:], t["w_x"]).then_inc(weights, 16)
            for b in range(NB):
                sp.dma_start(ctxT[:, b * NK * L:(b + 1) * NK * L], t["ctxT"][b]).then_inc(ctx_in, 16)
            with sp.Fori(0, NB) as b:
                for e in range(NE):
                    sp.wait_ge(gate_ready, b * NE + e + 1)
                    sp.dma_start(xz[:, e % 2], t["x"][bass.ds(b * L + e * P, P), :]).then_inc(x_in[e % 2], 16)
            sp.wait_ge(xd_out, 16 * NB + 16)
            for j in range(2):
                sp.wait_ge(ug_out[j], 16 * STEPS // 2 + 16)

        @block.gpsimd
        def _(pool):
            pool.memset(minus_half[:], -0.5).then_inc(exponent, 1)
            pool.wait_ge(exponent, 1)
            with pool.Fori(0, NB) as b:
                for e in range(NE):
                    pool.wait_ge(var_ready, b * NE + e + 1)
                    pool.tensor_tensor(out=rstd[:, e % 2:e % 2 + 1], in0=mv[:, e % 2, 1:2], in1=minus_half[:],
                                       op=ALU.pow).then_inc(rstd_ready, 1)

        @block.tensor
        def _(pe):
            pe.wait_ge(weights, 48)
            pe.wait_ge(ctx_in, 16 * NB)
            pe.sem_inc(xd_sums, 2)
            with pe.Fori(0, NB) as b:
                def x_dbl(e):
                    pe.wait_ge(u_ready, b * NE + e + 1)
                    if e == 0:
                        pe.wait_ge(xd_copied, b + 1)
                    for h in range(H2):
                        last = nc.tensor.matmul(halves(ps_d, h)[0:ND, :], w_x[:, e, :], halves(ug[:, e % 2, 0], h),
                                                start=e == 0, stop=e == NE - 1)
                    last.then_inc(xd_sums, 1)

                for e in range(NE):
                    pe.wait_ge(first_tap, b * NE + e + 1)
                    for h in range(H2):
                        for c in range(NK):
                            last = nc.tensor.matmul(halves(ps[e % 2], h), w_in[:, c, e * P:(e + 1) * P],
                                                    ctxT[:, bass.ds((b * NK + c) * L + h * HALF, HALF)],
                                                    start=c == 0, stop=c == NK - 1)
                    last.then_inc(projected, 1)
                    if e > 0:
                        x_dbl(e - 1)
                x_dbl(NE - 1)

        @block.scalar
        def _(act):
            act.sem_inc(first_tap, 2)
            act.sem_inc(gate_ready, 2)
            act.sem_inc(xd_copied, 1)
            act.sem_inc(xd_out, 16)
            for j in range(2):
                act.sem_inc(ug_out[j], 16)
            act.wait_ge(weights, 48)
            act.wait_ge(pads, 2)
            with act.Fori(0, NB) as b:
                for e in range(NE):
                    k, j = b * NE + e, e % 2
                    act.wait_ge(projected, k + 1)
                    act.wait_ge(taps, 3 * k + 3)
                    nc.scalar.activation(raw[:, j, TAPS - 1:], ps[j][:], ACT.Identity).then_inc(raw_copied, 1)
                    act.wait_ge(ug_out[j], 16 * (b * (NE // 2) + e // 2) + 16)
                    act.wait_ge(xd_sums, k + 1)
                    nc.scalar.activation(ug[:, j, 0], ps[j][:], ACT.Identity, bias=conv[:, e, TAPS:TAPS + 1],
                                         scale=conv[:, e, TAPS - 1:TAPS]).then_inc(first_tap, 1)
                    act.wait_ge(shift_ready, k + 1)
                    nc.scalar.activation(ug[:, j, 1], xz[:, j], ACT.Silu, bias=shift[:, j:j + 1],
                                         scale=rstd[:, j:j + 1]).then_inc(gate_ready, 1)
                    act.wait_ge(taps, 3 * k + 9)
                    nc.scalar.activation(ug[:, j, 0], ug[:, j, 0], ACT.Silu).then_inc(u_ready, 1)
                    act.wait_ge(u_ready, k + 1)
                    act.wait_ge(gate_ready, k + 3)
                    act.dma_start(t["ug"][bass.ds(k * P, P), :], ug[:, j].rearrange("p g l -> p (g l)")).then_inc(ug_out[j], 16)
                act.wait_ge(xd_sums, (b + 1) * NE + 2)
                act.wait_ge(xd_out, 16 * b + 16)
                nc.scalar.activation(xd[:], ps_d[0:ND, :], ACT.Copy).then_inc(xd_copied, 1)
                act.wait_ge(xd_copied, b + 2)
                act.dma_start(t["xd"][bass.ds(b * ND, ND), :], xd[:]).then_inc(xd_out, 16)

        @block.vector
        def _(dve):
            for j in range(2):
                nc.vector.memset(raw[:, j, 0:TAPS - 1], 0.0).then_inc(pads, 1)
            dve.sem_inc(taps, 6)
            dve.wait_ge(weights, 48)
            with dve.Fori(0, NB) as b:
                for e in range(NE):
                    k, j = b * NE + e, e % 2
                    chain = Chain(dve, stat_chain, 4 * k)
                    dve.wait_ge(x_in[j], 16 * (b * (NE // 2) + e // 2) + 16)
                    for h in range(H2):
                        chain.did(nc.vector.bn_stats(stats[:, j, 6 * h:6 * h + 6], halves(xz[:, j], h)))
                    chain.wait()
                    nc.vector.memset(carrier[:], 0.0)
                    chain.did(nc.vector.bn_aggr(mv[:, j], stats[:, j]))
                    chain.wait()
                    nc.vector.tensor_scalar(mv[:, j, 1:2], mv[:, j, 1:2], LN_EPS, None, ALU.add).then_inc(var_ready, 1)
                    dve.wait_ge(raw_copied, k + 1)
                    dve.wait_ge(first_tap, k + 3)
                    for i in range(TAPS - 1):
                        nc.vector.scalar_tensor_tensor(out=ug[:, j, 0], in0=raw[:, j, i:i + L], scalar=conv[:, e, i:i + 1],
                                                       in1=ug[:, j, 0], op0=ALU.mult, op1=ALU.add).then_inc(taps, 1)
                        if i == 0:
                            dve.wait_ge(rstd_ready, k + 1)
                            chain.did(nc.vector.scalar_tensor_tensor(
                                out=shift[:, j:j + 1], in0=mv[:, j, 0:1], scalar=-1.0, in1=rstd[:, j:j + 1],
                                op0=ALU.mult, op1=ALU.mult))
                            dve.wait_ge(stat_chain, 4 * k + 4)
                            nc.vector.sem_inc(shift_ready, 1)
                        if i < TAPS - 2:
                            dve.wait_ge(taps, 3 * k + 7 + i)


POOL_N = (4, 10)
VEC_N = tuple(n for n in range(NS) if n not in POOL_N)
HV = H2 * len(VEC_N)
LEAD = 3
SLOTS = 8
HC_SLOTS = 4


def sum_order():
    order = []
    for n in range(NS):
        if n in VEC_N:
            order.append(n)
        if n - 2 in POOL_N:
            order.append(n - 2)
    return order + [n for n in POOL_N if n not in order]


ORDER = sum_order()
assert ORDER[0] in VEC_N and ORDER[-1] in VEC_N + POOL_N and sorted(ORDER) == list(range(NS))
FIRST_TURN, LAST_TURN, MIDDLE = "first", "last", "middle"


def scan_stage(nc, t, ctx):
    def sb(name, shape):
        return ctx.enter_context(nc.sbuf_tensor("s_" + name, shape, F32))

    def sem(name):
        return nc.alloc_semaphore("s_" + name)

    bB = sb("bB", [P, NS, L])
    bC = sb("bC", [P, NS, L])
    delta = sb("delta", [P, 2, L])
    du = sb("du", [P, 2, L])
    u = sb("u", [P, L])
    gy = sb("gy", [P, L])
    xt = sb("xt", [P, L])
    dt = sb("dt", [NR, L])
    w = sb("w", [P, SLOTS, L])
    hc = sb("hc", [P, HC_SLOTS, HALF])
    ssm = sb("ssm", [P, 2, NS + 2])
    w_dt = sb("w_dt", [NR, 2, P])
    negA = sb("negA", [P, 2, NS])
    diagD = sb("diagD", [P, 2, P])
    ident = sb("ident", [P, P])
    tg_ident = sb("tg_ident", [P, P])
    tg = sb("tg", [P, 2])
    pA = [ctx.enter_context(nc.psum_tensor(f"s_pA{j}", [P, HALF], F32)) for j in range(2)]
    ph = [ctx.enter_context(nc.psum_tensor(f"s_ph{j}", [P, HALF], F32)) for j in range(2)]
    py = ctx.enter_context(nc.psum_tensor("s_py", [P, L], F32))
    pm = ctx.enter_context(nc.psum_tensor("s_pm", [P, L], F32))

    g_in, consts, made = sem("g_in"), sem("consts"), sem("made")
    u_in, rest_in, dt_in = [sem(f"u_in{j}") for j in range(2)], sem("rest_in"), sem("dt_in")
    B_in, C_in = [sem(f"B_in{g}") for g in range(4)], [sem(f"C_in{g}") for g in range(4)]
    dt_done, dt_read, act_chain, soft_ready = sem("dt_done"), sem("dt_read"), sem("act_chain"), sem("soft_ready")
    delta_ready, du_ready, diag_ready = sem("delta_ready"), sem("du_ready"), sem("diag_ready")
    dA_ready, w_ready, scanned = sem("dA_ready"), sem("w_ready"), sem("scanned")
    vec_hc, pool_hc, summed, skip_done = sem("vec_hc"), sem("pool_hc"), sem("summed"), sem("skip_done")
    y_used, transposed, x2_ready, stored = sem("y_used"), sem("transposed"), sem("x2_ready"), sem("stored")

    xd, GROUP = t["xd"], NS // 4
    place = {n: i for i, n in enumerate(ORDER)}

    def summed_after(k, n, h=H2 - 1):
        return H2 * (NS * (k + 1) + place[n]) + h + 1

    def turns(eng, step):
        step(0, 0, FIRST_TURN)
        step(1, 1, MIDDLE)
        with eng.Fori(1, STEPS // 2 - 1) as i:
            for j in range(2):
                step(2 * i + j, j, MIDDLE)
        step(STEPS - 2, 0, MIDDLE)
        step(STEPS - 1, 1, LAST_TURN)

    def of_pair(k):
        return 64 * (k // 2) + 64

    def of_batch(k):
        return 16 * (k // NE) + 16

    with nc.Block() as block:
        @block.sync
        def _(sp):
            sp.dma_start(tg[:], t["g"].partition_broadcast(P)).then_inc(g_in, 16)

            def load_start(b, e, j):
                k = b * NE + e
                sp.wait_ge(dt_done, k + 1)
                sp.dma_start(ssm[:, j], t["ssm"][bass.ds(e * P, P), :]).then_inc(u_in[j], 16)
                sp.dma_start(w_dt[:, j], t["w_dt"][bass.ds(e * NR, NR), :]).then_inc(u_in[j], 16)
                sp.dma_start(dt[:], xd[bass.ds(b * ND, NR), :]).then_inc(u_in[j], 16)
                sp.wait_ge(skip_done, k + 1)
                sp.dma_start(u[:], t["ug"][bass.ds(k * P, P), 0:L]).then_inc(u_in[j], 16)

            def load_BC(b):
                for g in range(4):
                    if not isinstance(b, int):
                        last = max(range(g * GROUP, (g + 1) * GROUP), key=lambda n: place[n])
                        sp.wait_ge(summed, summed_after(b * NE - 1, last))
                    for dst, o, arrived in ((bB, NR, B_in), (bC, NR + NS, C_in)):
                        rows = xd[bass.ds(b * ND + o + g * GROUP, GROUP), :]
                        sp.dma_start(dst[:, g * GROUP:(g + 1) * GROUP],
                                     rows.partition_broadcast(P)).then_inc(arrived[g], 16)

            def store(b, e):
                sp.wait_ge(x2_ready, b * NE + e + 1)
                sp.dma_start(t["x2"][bass.ds(b * L, L), bass.ds(e * P, P)].rearrange("(a p) c -> p a c", p=P),
                             xt[:].rearrange("p (a c) -> p a c", c=P)).then_inc(stored, 16)

            def load_end(b, e):
                k = b * NE + e
                sp.wait_ge(stored, 16 * k + 16)
                sp.dma_start(gy[:], t["ug"][bass.ds(k * P, P), L:2 * L]).then_inc(rest_in, 16)
                sp.dma_start(xt[:].rearrange("p (a c) -> p a c", c=P),
                             t["x"][bass.ds(b * L, L), bass.ds(e * P, P)].rearrange("(a p) c -> p a c", p=P)).then_inc(rest_in, 16)

            def batch(b):
                load_start(b, 0, 0)
                load_BC(b)
                if not isinstance(b, int):
                    store(b - 1, NE - 1)
                load_end(b, 0)
                load_start(b, 1, 1)
                store(b, 0)
                load_end(b, 1)
                with sp.Fori(1, NE // 2) as i:
                    for j in range(2):
                        load_start(b, 2 * i + j, j)
                        store(b, 2 * i + j - 1)
                        load_end(b, 2 * i + j)

            batch(0)
            with sp.Fori(1, NB) as b:
                batch(b)
            store(NB - 1, NE - 1)
            sp.wait_ge(stored, 16 * STEPS + 16)

        @block.gpsimd
        def _(pool):
            pool.memset(ident[:], 0.0).then_inc(made, 1)
            pool.wait_ge(made, 1)
            pool.affine_select(out=ident[:], in_=ident[:], compare_op=ALU.not_equal, fill=1.0, base=0,
                               pattern=[[-1, P]], channel_multiplier=1).then_inc(made, 1)

            def make_w(k, n, j):
                if n >= NS:
                    k, n, j = k + 1, n - NS, 1 - j
                if n == 0:
                    pool.wait_ge(du_ready, k + 1)
                if n % GROUP == 0:
                    pool.wait_ge(B_in[n // GROUP], of_batch(k))
                m = n - SLOTS
                pool.wait_ge(summed, summed_after(k, m) if m >= 0 else summed_after(k - 1, m + NS))
                pool.tensor_tensor(out=w[:, n % SLOTS], in0=du[:, j], in1=bB[:, n], op=ALU.mult).then_inc(w_ready, 1)

            def times_C(k, n):
                if n in POOL_N:
                    pool.wait_ge(scanned, H2 * (NS * k + n + 1) + 2)
                    pool.wait_ge(C_in[n // GROUP], of_batch(k))
                    pool.tensor_tensor(out=w[:, n % SLOTS], in0=w[:, n % SLOTS], in1=bC[:, n],
                                       op=ALU.mult).then_inc(pool_hc, 1)

            def step(k, j, turn):
                if turn == FIRST_TURN:
                    for n in range(LEAD):
                        make_w(k, n, j)
                for n in range(NS):
                    if turn != LAST_TURN or n + LEAD < NS:
                        make_w(k, n + LEAD, j)
                    if n > 0:
                        times_C(k, n - 1)
                times_C(k, NS - 1)
            turns(pool, step)

        @block.tensor
        def _(pe):
            pe.wait_ge(consts, 1)
            pe.sem_inc(summed, H2 * NS)
            pe.sem_inc(dt_done, 1)
            pe.sem_inc(skip_done, 1)

            def dt_proj(k, j, first):
                pe.wait_ge(u_in[j], of_pair(k))
                if not first:
                    pe.wait_ge(x2_ready, k - 1)
                for h in range(H2):
                    last = nc.tensor.matmul(halves(pm, h), w_dt[:, j], halves(dt, h), start=True, stop=True)
                last.then_inc(dt_done, 1)

            def finish(k, is_last):
                pe.wait_ge(y_used, k + 1)
                pe.wait_ge(rest_in, 32 * k + 32)
                pe.wait_ge(dt_read, k + 1 if is_last else k + 2)
                for h in range(H2):
                    nc.tensor.matmul(halves(pm, h), ident[:], halves(xt, h), start=True, stop=False)
                    for a in range(HALF // P):
                        c = slice(h * HALF + a * P, h * HALF + (a + 1) * P)
                        last = nc.tensor.matmul(pm[:, c], gy[:, c], tg_ident[:], start=False, stop=a == HALF // P - 1)
                last.then_inc(transposed, 1)

            def step(k, j, turn):
                if turn == FIRST_TURN:
                    dt_proj(k, j, True)
                else:
                    finish(k - 1, False)
                pe.wait_ge(diag_ready, k + 1)
                pe.wait_ge(du_ready, k + 1)
                for h in range(H2):
                    last = nc.tensor.matmul(halves(py, h), diagD[:, j], halves(u, h), start=True, stop=False)
                last.then_inc(skip_done, 1)
                vec, pooled = 0, 0
                for at, n in enumerate(ORDER):
                    if n in POOL_N:
                        pooled += 1
                        pe.wait_ge(pool_hc, len(POOL_N) * k + pooled)
                    for h in range(H2):
                        if n in VEC_N:
                            pe.wait_ge(vec_hc, HV * k + vec + 2)
                            product = hc[:, vec % HC_SLOTS]
                            vec += 1
                        else:
                            product = halves(w[:, n % SLOTS], h)
                        nc.tensor.matmul(halves(py, h), ident[:], product, start=False, stop=at == NS - 1).then_inc(summed, 1)
                    if at == 6 and turn != LAST_TURN:
                        dt_proj(k + 1, 1 - j, turn == FIRST_TURN)
                if turn == LAST_TURN:
                    finish(k, True)
            turns(pe, step)

        @block.scalar
        def _(act):
            act.wait_ge(g_in, 16)
            nc.scalar.activation(tg[:], tg[:], ACT.Tanh).then_inc(act_chain, 1)
            act.wait_ge(act_chain, 1)
            act.wait_ge(made, 2)
            nc.scalar.activation(tg_ident[:], ident[:], ACT.Copy, scale=tg[:, 0:1]).then_inc(consts, 1)
            act.sem_inc(stored, 16)

            def softplus(k, j):
                chain = Chain(act, act_chain, 3 * k + 1)
                act.wait_ge(u_in[j], of_pair(k))
                act.wait_ge(dt_done, k + 2)
                bias = ssm[:, j, NS:NS + 1]
                nc.scalar.activation(du[:, j], pm[:], ACT.Relu, bias=bias)
                nc.scalar.activation(delta[:, j], pm[:], ACT.Abs, bias=bias).then_inc(dt_read, 1)
                chain.did(nc.scalar.activation(negA[:, j], ssm[:, j, 0:NS], ACT.Exp))
                chain.did(nc.scalar.activation(diagD[:, j], ident[:], ACT.Copy, scale=ssm[:, j, NS + 1:NS + 2]))
                act.wait_ge(dt_read, k + 1)
                chain.did(nc.scalar.activation(delta[:, j], delta[:, j], ACT.Exp, scale=-1.0))
                chain.wait()
                nc.scalar.activation(delta[:, j], delta[:, j], ACT.Ln, bias=1.0).then_inc(soft_ready, 1)
                nc.scalar.activation(negA[:, j], negA[:, j], ACT.Copy, scale=-1.0).then_inc(diag_ready, 1)

            def finish(k):
                act.wait_ge(transposed, k + 1)
                nc.scalar.activation(xt[:], pm[:], ACT.Copy).then_inc(x2_ready, 1)

            def step(k, j, turn):
                if turn == FIRST_TURN:
                    softplus(k, j)
                act.wait_ge(diag_ready, k + 1)
                act.wait_ge(delta_ready, k + 1)
                for q in range(H2 * NS):
                    n, h = q // H2, q % H2
                    act.wait_ge(scanned, H2 * NS * k + q + 1)
                    nc.scalar.activation(pA[h][:], halves(delta[:, j], h), ACT.Exp,
                                         scale=negA[:, j, n:n + 1]).then_inc(dA_ready, 1)
                    if q == 8 and turn != FIRST_TURN:
                        finish(k - 1)
                    if q == 17 and turn != LAST_TURN:
                        softplus(k + 1, 1 - j)
                if turn == LAST_TURN:
                    finish(k)
            turns(act, step)

        @block.vector
        def _(dve):
            dve.sem_inc(scanned, 2)
            dve.sem_inc(vec_hc, 1)

            def start(k, j):
                dve.wait_ge(soft_ready, k + 1)
                nc.vector.tensor_tensor(delta[:, j], delta[:, j], du[:, j], ALU.add).then_inc(delta_ready, 1)
                dve.wait_ge(delta_ready, k + 1)
                dve.wait_ge(u_in[j], of_pair(k))
                nc.vector.tensor_tensor(du[:, j], delta[:, j], u[:], ALU.mult).then_inc(du_ready, 1)

            def gate(k):
                dve.wait_ge(summed, H2 * NS * (k + 2))
                dve.wait_ge(rest_in, 32 * k + 32)
                nc.vector.tensor_tensor(gy[:], py[:], gy[:], ALU.mult).then_inc(y_used, 1)

            def step(k, j, turn):
                if turn == FIRST_TURN:
                    start(k, j)
                vec = 0

                def times_C(q):
                    nonlocal vec
                    n, h = q // H2, q % H2
                    if n not in VEC_N:
                        return
                    dve.wait_ge(scanned, H2 * NS * k + q + 3)
                    if h == 0 and n == min(m for m in VEC_N if m // GROUP == n // GROUP):
                        dve.wait_ge(C_in[n // GROUP], of_batch(k))
                    m = VEC_N.index(n) - HC_SLOTS // H2
                    dve.wait_ge(summed, summed_after(k, VEC_N[m], h) if m >= 0 else summed_after(k - 1, VEC_N[m], h))
                    nc.vector.tensor_tensor(hc[:, vec % HC_SLOTS], ph[h][:], halves(bC[:, n], h), ALU.mult).then_inc(vec_hc, 1)
                    vec += 1

                for q in range(H2 * NS):
                    n, h = q // H2, q % H2
                    out = ph[h][:] if n in VEC_N else halves(w[:, n % SLOTS], h)
                    dve.wait_ge(dA_ready, H2 * NS * k + q + 1)
                    if h == 0:
                        dve.wait_ge(w_ready, NS * k + n + 1)
                        initial = 0.0
                    else:
                        dve.wait_ge(scanned, H2 * NS * k + q + 2)
                    if n in VEC_N:
                        dve.wait_ge(vec_hc, HV * k + vec + 1)
                    nc.vector.tensor_tensor_scan(out, pA[h][:], halves(w[:, n % SLOTS], h), initial,
                                                 ALU.mult, ALU.add).then_inc(scanned, 1)
                    initial = out[:, HALF - 1:HALF]
                    if q > 0:
                        times_C(q - 1)
                    if q == 3 and turn != FIRST_TURN:
                        gate(k - 1)
                    if q == 23 and turn != LAST_TURN:
                        start(k + 1, 1 - j)
                times_C(H2 * NS - 1)
                if turn == LAST_TURN:
                    gate(k)
            turns(dve, step)


def route_stage(nc, t, ctx):
    TILES, BUFS = L // P, 8

    def sb(name, shape):
        return ctx.enter_context(nc.sbuf_tensor("r_" + name, shape, F32))

    def sem(name):
        return nc.alloc_semaphore("r_" + name)

    x2 = sb("x2", [P, BUFS, DI])
    ln = sb("ln", [P, BUFS, DI])
    tgln = sb("tgln", [P, BUFS, DI])
    router = sb("router", [P, DI])
    tg = sb("tg", [P, 2])
    counts = sb("counts", [P, P + TILES])
    stats = sb("stats", [P, BUFS, H2 * 6])
    mv = sb("mv", [P, BUFS, 2])
    rstd = sb("rstd", [P, BUFS])
    shift = sb("shift", [P, BUFS])
    minus_half = sb("minus_half", [P, 1])
    carrier = sb("carrier", [P, 1])
    score = sb("score", [P, TILES])
    ident = sb("ident", [P, P])
    ones = sb("ones", [P, P])
    before = sb("before", [P, P])
    WIDE = (TILES - 1) * P
    earlier = sb("earlier", [P, WIDE + L])
    diag = sb("diag", [P, TILES, P])
    row = sb("row", [P, L])
    scrap = sb("scrap", [P, L])
    own = sb("own", [P, TILES])
    larger = sb("larger", [P, TILES])
    equal = sb("equal", [P, TILES])
    chosen = sb("chosen", [P, TILES])
    sums = sb("sums", [P, 2 * TILES])
    upto = sb("upto", [P, TILES])
    slot = sb("slot", [P, TILES])
    pick = sb("pick", [P, TILES, P])
    pos = sb("pos", [P, NB])
    p_row = ctx.enter_context(nc.psum_tensor("r_prow", [P, L], F32))
    p_sums = ctx.enter_context(nc.psum_tensor("r_psums", [P, 2 * TILES], F32))
    p_pos = ctx.enter_context(nc.psum_tensor("r_ppos", [P, 1], F32))

    small, x_in, out_done = sem("small"), [sem(f"x_in{j}") for j in range(BUFS)], [sem(f"out{j}") for j in range(BUFS)]
    masks, stat_chain, var_ready, rstd_ready, shift_ready = sem("masks"), sem("stat"), sem("var"), sem("rstd_r"), sem("shift_r")
    ln_ready, tgln_ready, scored, base_ready, tg_ready = sem("ln_r"), sem("tgln_r"), sem("scored"), sem("base"), sem("tg_r")
    diag_ready, row_sums, row_ready, chosen_ready = sem("diag_r"), sem("row_sums"), sem("row_r"), sem("chosen_r")
    slot_sums, rank_chain, pick_ready, pos_sums, pos_done = sem("slot_sums"), sem("rank"), sem("pick_r"), sem("pos_sums"), sem("pos_done")

    with nc.Block() as block:
        @block.sync
        def _(sp):
            sp.dma_start(router[:], t["router"].partition_broadcast(P)).then_inc(small, 16)
            sp.dma_start(tg[:], t["g"].partition_broadcast(P)).then_inc(small, 16)
            sp.dma_start(counts[:], t["counts"]).then_inc(small, 16)
            with sp.Fori(0, NB) as b:
                for a in range(TILES):
                    sp.wait_ge(out_done[a % BUFS], 16 * (b * (TILES // BUFS) + a // BUFS) + 16)
                    sp.dma_start(x2[:, a % BUFS], t["x2"][bass.ds(b * L + a * P, P), :]).then_inc(x_in[a % BUFS], 16)
            sp.wait_ge(pos_done, NB)
            sp.dma_start(t["pos"], pos[:]).then_inc(small, 16)
            sp.wait_ge(small, 64)
            for j in range(BUFS):
                sp.wait_ge(out_done[j], 16 * NB * (TILES // BUFS) + 16)

        @block.gpsimd
        def _(pool):
            pool.memset(minus_half[:], -0.5).then_inc(masks, 1)
            pool.memset(ident[:], 0.0).then_inc(masks, 1)
            pool.memset(before[:], 1.0).then_inc(masks, 1)
            pool.memset(earlier[:], 1.0).then_inc(masks, 1)
            pool.memset(ones[:], 1.0).then_inc(masks, 1)
            pool.wait_ge(masks, 5)
            pool.affine_select(out=ident[:], in_=ident[:], compare_op=ALU.not_equal, fill=1.0, base=0,
                               pattern=[[-1, P]], channel_multiplier=1).then_inc(masks, 1)
            pool.affine_select(out=before[:], in_=before[:], compare_op=ALU.is_gt, fill=0.0, base=0,
                               pattern=[[1, P]], channel_multiplier=-1).then_inc(masks, 1)
            pool.affine_select(out=earlier[:], in_=earlier[:], compare_op=ALU.is_gt, fill=0.0, base=WIDE,
                               pattern=[[-1, WIDE + L]], channel_multiplier=1).then_inc(masks, 1)
            with pool.Fori(0, NB) as b:
                for a in range(TILES + 2):
                    if a < TILES:
                        j = a % BUFS
                        pool.wait_ge(var_ready, b * TILES + a + 1)
                        pool.tensor_tensor(out=rstd[:, j:j + 1], in0=mv[:, j, 1:2], in1=minus_half[:],
                                           op=ALU.pow).then_inc(rstd_ready, 1)
                    if a >= 2:
                        j = (a - 2) % BUFS
                        pool.wait_ge(tgln_ready, b * TILES + a - 1)
                        pool.tensor_tensor(out=tgln[:, j], in0=tgln[:, j], in1=x2[:, j], op=ALU.add).then_inc(base_ready, 1)

        @block.scalar
        def _(act):
            for j in range(BUFS):
                act.sem_inc(out_done[j], 16)
            act.sem_inc(scored, BUFS)
            act.wait_ge(small, 48)
            nc.scalar.activation(tg[:], tg[:], ACT.Tanh).then_inc(tg_ready, 1)
            act.wait_ge(tg_ready, 1)
            with act.Fori(0, NB) as b:
                for a in range(TILES + 3):
                    if a >= 3:
                        j = (a - 3) % BUFS
                        act.wait_ge(base_ready, b * TILES + a - 2)
                        act.dma_start(t["out"][bass.ds(b * L + (a - 3) * P, P), :], tgln[:, j]).then_inc(out_done[j], 16)
                    if a < TILES:
                        j, k = a % BUFS, b * TILES + a
                        act.wait_ge(shift_ready, k + 1)
                        act.wait_ge(scored, k + 1)
                        nc.scalar.activation(ln[:, j], x2[:, j], ACT.Identity, bias=shift[:, j:j + 1],
                                             scale=rstd[:, j:j + 1]).then_inc(ln_ready, 1)
                        act.wait_ge(ln_ready, k + 1)
                        act.wait_ge(out_done[j], 16 * (b * (TILES // BUFS) + a // BUFS) + 16)
                        nc.scalar.activation(tgln[:, j], ln[:, j], ACT.Copy, scale=tg[:, 1:2]).then_inc(tgln_ready, 1)
                act.wait_ge(row_sums, b + 1)
                nc.scalar.activation(row[:], p_row[:], ACT.Copy).then_inc(row_ready, 1)

        @block.tensor
        def _(pe):
            pe.wait_ge(masks, 8)
            with pe.Fori(0, NB) as b:
                pe.wait_ge(diag_ready, b + 1)
                for a in range(TILES):
                    last = nc.tensor.matmul(p_row[:, a * P:(a + 1) * P], ones[:], diag[:, a], start=True, stop=True)
                last.then_inc(row_sums, 1)
                pe.wait_ge(chosen_ready, b + 1)
                nc.tensor.matmul(p_sums[:, 0:TILES], before[:], chosen[:], start=True, stop=True)
                nc.tensor.matmul(p_sums[:, TILES:], ones[:], chosen[:], start=True, stop=True).then_inc(slot_sums, 1)
                pe.wait_ge(pick_ready, b + 1)
                for a in range(TILES):
                    last = nc.tensor.matmul(p_pos[:], pick[:, a], counts[:, P + a:P + a + 1], start=a == 0, stop=a == TILES - 1)
                last.then_inc(pos_sums, 1)

        @block.vector
        def _(dve):
            dve.wait_ge(small, 48)
            dve.wait_ge(masks, 8)
            with dve.Fori(0, NB) as b:
                chain = Chain(dve, stat_chain, b * TILES * 3)
                for a in range(TILES + 2):
                    if a < TILES:
                        j, k = a % BUFS, b * TILES + a
                        dve.wait_ge(x_in[j], 16 * (b * (TILES // BUFS) + a // BUFS) + 16)
                        for h in range(H2):
                            chain.did(nc.vector.bn_stats(stats[:, j, 6 * h:6 * h + 6], halves(x2[:, j], h)))
                        chain.wait()
                        nc.vector.memset(carrier[:], 0.0)
                        chain.did(nc.vector.bn_aggr(mv[:, j], stats[:, j]))
                        chain.wait()
                        nc.vector.tensor_scalar(mv[:, j, 1:2], mv[:, j, 1:2], LN_EPS, None, ALU.add).then_inc(var_ready, 1)
                    if 1 <= a <= TILES:
                        j = (a - 1) % BUFS
                        dve.wait_ge(rstd_ready, b * TILES + a)
                        nc.vector.scalar_tensor_tensor(out=shift[:, j:j + 1], in0=mv[:, j, 0:1], scalar=-1.0,
                                                       in1=rstd[:, j:j + 1], op0=ALU.mult, op1=ALU.mult).then_inc(shift_ready, 1)
                    if a >= 2:
                        j = (a - 2) % BUFS
                        dve.wait_ge(tgln_ready, b * TILES + a - 1)
                        nc.vector.tensor_tensor_reduce(out=ln[:, j], in0=ln[:, j], in1=router[:], scale=1.0, scalar=0.0,
                                                       op0=ALU.mult, op1=ALU.add,
                                                       accum_out=score[:, a - 2:a - 1]).then_inc(scored, 1)
                dve.wait_ge(scored, (b + 1) * TILES + BUFS)
                rank = Chain(dve, rank_chain, b * RANK_STEPS)
                for a in range(TILES):
                    last = nc.vector.tensor_scalar(diag[:, a], ident[:], score[:, a:a + 1], None, ALU.mult)
                last.then_inc(diag_ready, 1)
                dve.wait_ge(row_ready, b + 1)
                for a in range(TILES):
                    if a:
                        rank.wait()
                    rank.did(nc.vector.tensor_tensor_reduce(out=scrap[:, 0:P], in0=row[:, a * P:(a + 1) * P], in1=ident[:],
                                                            scale=1.0, scalar=0.0, op0=ALU.mult, op1=ALU.add,
                                                            accum_out=own[:, a:a + 1]))
                for a in range(TILES):
                    rank.wait()
                    rank.did(nc.vector.tensor_scalar(scrap[:], row[:], own[:, a:a + 1], None, ALU.is_gt, ALU.add,
                                                     accum_out=larger[:, a:a + 1]))
                    rank.wait()
                    rank.did(nc.vector.scalar_tensor_tensor(out=scrap[:], in0=row[:], scalar=own[:, a:a + 1],
                                                            in1=earlier[:, WIDE - a * P:WIDE - a * P + L],
                                                            op0=ALU.is_equal, op1=ALU.mult, accum_out=equal[:, a:a + 1]))
                rank.wait()
                rank.did(nc.vector.tensor_tensor(larger[:], larger[:], equal[:], ALU.add))
                rank.wait()
                nc.vector.tensor_scalar(chosen[:], larger[:], float(TOPK), None, ALU.is_lt).then_inc(chosen_ready, 1)
                dve.wait_ge(slot_sums, b + 1)
                rank.did(nc.vector.tensor_copy(sums[:], p_sums[:]))
                rank.wait()
                rank.did(nc.vector.tensor_tensor_scan(upto[:], ones[:, 0:TILES], sums[:, TILES:], 0.0, ALU.mult, ALU.add))
                rank.wait()
                rank.did(nc.vector.tensor_tensor(slot[:], upto[:], sums[:, TILES:], ALU.subtract))
                rank.wait()
                rank.did(nc.vector.tensor_tensor(slot[:], slot[:], sums[:, 0:TILES], ALU.add))
                rank.wait()
                dve.wait_ge(chosen_ready, b + 1)
                for a in range(TILES):
                    last = nc.vector.tensor_scalar(pick[:, a], counts[:, 0:P], slot[:, a:a + 1], chosen[:, a:a + 1],
                                                   ALU.is_equal, ALU.mult)
                last.then_inc(pick_ready, 1)
                dve.wait_ge(pos_sums, b + 1)
                nc.vector.tensor_copy(pos[:, bass.ds(b, 1)], p_pos[:]).then_inc(pos_done, 1)
                assert rank.n == RANK_STEPS and chain.n == 3 * TILES


RANK_STEPS = 3 * (L // P) + 5


def layer_stage(nc, t, ctx):
    SLOTS_W, KT = 8, DI // P
    QK = NH + NKV
    SCALE = float(DH) ** -0.5
    MASKED = -1.0e30

    def sb(name, shape, dtype=F32):
        return ctx.enter_context(nc.sbuf_tensor("l_" + name, shape, dtype))

    def sem(name):
        return nc.alloc_semaphore("l_" + name)

    rows = sb("rows", [P, NB, DI])
    hid = sb("hid", [P, NB * DI])
    branch = hid[:].rearrange("p (m s) -> p m s", s=S)
    xT = sb("xT", [P, KT, S])
    hT = sb("hT", [P, KT, S])
    big = sb("big", [P, NI * S])
    v = big[:, QK * S:]
    ring = sb("ring", [P, SLOTS_W, KT, P])
    work = sb("work", [P, 14, S])
    rms = sb("rms", [P, S])
    minus_half = sb("minus_half", [P, S])
    ropes = sb("ropes", [P, NB, 2 * DH])
    rope = sb("rope", [P, 2, S])
    cols = sb("cols", [P, 2 * NKV + NH + 2 * KT])
    ident = sb("ident", [P, P])
    ones = sb("ones", [P, P])
    causal = sb("causal", [P, P])
    swap = sb("swap", [P, P])
    router = sb("router", [P, DI])
    tg = sb("tg", [P, 2])
    pos = sb("pos", [P, NB])
    pos_i = sb("pos_i", [P, NB], I32)
    row_f = sb("row_f", [P, NB])
    row_i = sb("row_i", [P, NB], I32)
    stats = sb("stats", [P, NB, H2 * 6])
    mv = sb("mv", [P, NB, 2])
    rstd = sb("rstd", [P, NB])
    shift = sb("shift", [P, NB])
    score = sb("score", [P, NB])
    coef = sb("coef", [P, NB])
    carrier = sb("carrier", [P, 1])
    top = sb("top", [P, 4])
    bias = sb("bias", [P, 4])
    total = sb("total", [P, 4])
    inv = sb("inv", [P, 4])
    banks = [ctx.enter_context(nc.psum_tensor(f"l_p{j}", [P, S], F32)) for j in range(8)]
    acc, side = banks[0:4], banks[4:8]

    raw, part_c, part_s = work[:, 0:2], work[:, 2:4], work[:, 4:6]
    square, silu = work[:, 6:10], work[:, 10:12]
    prob, probT, q2, v1, k1 = work[:, 0:4], work[:, 4:6], work[:, 6:10], work[:, 10:12], work[:, 12:14]

    small, made, pos_in, idx_ready = sem("small"), sem("made"), sem("pos_in"), sem("idx")
    x_in, rope_in = ([sem(f"{n}_in{b}") for b in range(NB)] for n in ("x", "rope"))
    chain_s, var_ready, rstd_ready, shift_ready, hid_ready, base_ready = (sem(n) for n in ("chain", "var", "rstd_r", "shift_r", "hid_r", "base_r"))
    score_ready, e_ready, coef_ready, tg_ready = sem("score_r"), sem("e_r"), sem("coef_r"), sem("tg_r")
    turned, turned_out, rope_turned, rope_ready = sem("turned"), sem("turned_out"), sem("rope_turned"), sem("rope_r")
    square_ready, square_used, mean_ready, pow_ready, h_ready = sem("square_r"), sem("square_u"), sem("mean_r"), sem("pow_r"), sem("h_r")
    w_in, w_used = [sem(f"w_in{j}") for j in range(SLOTS_W)], sem("w_used")
    lin, raw_ready, rotated, cos_part, sin_part, qk_ready = sem("lin"), sem("raw_r"), sem("rotated"), sem("cos_p"), sem("sin_p"), sem("qk_r")
    v_turned, v_ready = sem("v_turned"), sem("v_r")
    staged, scores, topped, biased, expd, inverted, normed = (sem(n) for n in ("staged", "scores", "topped", "biased", "expd", "inverted", "normed"))
    p_turned, probT_ready, o_done, o_ready = sem("p_turned"), sem("probT_r"), sem("o_done"), sem("o_r")
    wo_done, attn_ready, x1_ready = sem("wo_done"), sem("attn_r"), sem("x1_r")
    gate_done, up_done, silu_ready, act_ready = sem("gate_d"), sem("up_d"), sem("silu_r"), sem("act_r")
    down_done, branch_ready, back, rows_ready, scattered = sem("down_d"), sem("branch_r"), sem("back"), sem("rows_r"), [sem(f"scattered{b}") for b in range(NB)]

    U_WO, U_MLP, U_DOWN, U_END = QK + NKV, QK + NKV + 2 * KT, QK + NKV + 2 * KT + 2 * NI, QK + NKV + 2 * KT + 2 * NI + 4 * KT
    KV2 = NKV // 2
    COMBOS = 4 * NB

    with nc.Block() as block:
        @block.sync
        def _(sp):
            sp.dma_start(pos[:], t["pos"]).then_inc(pos_in, 16)
            for dst, src in ((cols, t["cols"]), (swap, t["swap"]), (router, t["router"].partition_broadcast(P)),
                             (tg, t["g"].partition_broadcast(P))):
                sp.dma_start(dst[:], src).then_inc(small, 16)

            def load(i8, j, src):
                sp.wait_ge(w_used, i8 * SLOTS_W + j + 1)
                sp.dma_start(ring[:, j].rearrange("p k c -> p (k c)"), src).then_inc(w_in[j], 16)

            with sp.Fori(0, NH // SLOTS_W) as i:
                for j in range(SLOTS_W):
                    load(i, j, t["wq"][bass.ds((i * SLOTS_W + j) * P, P), :])
            for n, name in enumerate(("wk", "wv")):
                for j in range(SLOTS_W):
                    load(NH // SLOTS_W + n, j, t[name][j * P:(j + 1) * P, :])
            for i in range(2):
                for j in range(SLOTS_W):
                    m, part = (i * SLOTS_W + j) // 2, j % 2
                    load(U_WO // SLOTS_W + i, j, t["wo"][m * P:(m + 1) * P, part * KT * P:(part + 1) * KT * P])
            with sp.Fori(0, NI // 4) as i:
                for j in range(SLOTS_W):
                    name = ("w_gate", "w_up")[j % 2]
                    load(i + U_MLP // SLOTS_W, j, t[name][bass.ds((i * 4 + j // 2) * P, P), :])
            with sp.Fori(0, KT // 2) as i:
                for j in range(SLOTS_W):
                    part = j % 4
                    load(i + U_DOWN // SLOTS_W, j, t["w_down"][bass.ds((i * 2 + j // 4) * P, P), part * KT * P:(part + 1) * KT * P])
            for b in range(NB):
                sp.wait_ge(scattered[b], 16)

        @block.gpsimd
        def _(pool):
            pool.memset(minus_half[:], -0.5).then_inc(made, 1)
            pool.memset(ident[:], 0.0).then_inc(made, 1)
            pool.memset(causal[:], 0.0).then_inc(made, 1)
            pool.memset(ones[:], 1.0).then_inc(made, 1)
            pool.wait_ge(made, 4)
            pool.affine_select(out=ident[:], in_=ident[:], compare_op=ALU.not_equal, fill=1.0, base=0,
                               pattern=[[-1, P]], channel_multiplier=1).then_inc(made, 1)
            pool.affine_select(out=causal[:], in_=causal[:], compare_op=ALU.is_ge, fill=MASKED, base=0,
                               pattern=[[-1, P]], channel_multiplier=1).then_inc(made, 1)
            pool.wait_ge(idx_ready, 2)
            for b in range(NB):
                pool.indirect_dma_start(out=rows[:, b], out_offset=None, in_=t["x2"],
                                        in_offset=bass.IndirectOffsetOnAxis(ap=row_i[:, b:b + 1], axis=0)).then_inc(x_in[b], 16)
            for b in range(NB):
                pool.indirect_dma_start(out=ropes[:, b], out_offset=None, in_=t["rope"],
                                        in_offset=bass.IndirectOffsetOnAxis(ap=pos_i[:, b:b + 1], axis=0)).then_inc(rope_in[b], 16)
            pool.wait_ge(var_ready, 1)
            pool.tensor_tensor(out=rstd[:], in0=mv[:, :, 1], in1=minus_half[:, 0:NB], op=ALU.pow).then_inc(rstd_ready, 1)
            for r in range(2):
                pool.wait_ge(mean_ready, r + 1)
                pool.tensor_tensor(out=rms[:], in0=rms[:], in1=minus_half[:], op=ALU.pow).then_inc(pow_ready, 1)
            for b in range(NB):
                pool.wait_ge(rows_ready, b + 1)
                pool.indirect_dma_start(out=t["out"], out_offset=bass.IndirectOffsetOnAxis(ap=row_i[:, b:b + 1], axis=0),
                                        in_=rows[:, b], in_offset=None).then_inc(scattered[b], 16)

        @block.tensor
        def _(pe):
            pe.wait_ge(made, 6)
            pe.wait_ge(small, 64)
            pe.sem_inc(w_used, SLOTS_W)
            pe.sem_inc(square_used, 4)
            pe.sem_inc(rotated, 2)
            pe.sem_inc(p_turned, 4)
            pe.sem_inc(o_done, COMBOS)

            def unit(i8, j, out, rhs, start, stop):
                pe.wait_ge(w_in[j], 16 * (i8 + 1))
                for c in range(KT):
                    last = nc.tensor.matmul(out[:], ring[:, j, c], rhs(c), start=start and c == 0, stop=stop and c == KT - 1)
                last.then_inc(w_used, 1)
                return last

            def mean_squares(r):
                for c in range(KT):
                    pe.wait_ge(square_ready, r * KT + c + 1)
                    last = nc.tensor.matmul(side[0][:], ones[:], square[:, c % 4], start=c == 0, stop=c == KT - 1)
                    last.then_inc(square_used, 1)

            pe.wait_ge(hid_ready, NB)
            for c in range(KT):
                if c >= 4:
                    pe.wait_ge(square_ready, c - 3)
                for b in range(NB):
                    last = nc.tensor.matmul(acc[c % 4][:, b * P:(b + 1) * P], hid[:, b * DI + c * P:b * DI + (c + 1) * P],
                                            ident[:], start=b == 0, stop=b == NB - 1)
                last.then_inc(turned, 1)
            for r in range(2):
                for b in range(NB):
                    pe.wait_ge(rope_in[b], 16)
                    last = nc.tensor.matmul(side[2 + r][:, b * P:(b + 1) * P], ropes[:, b, r * DH:(r + 1) * DH], ident[:],
                                            start=b == 0, stop=b == NB - 1)
                last.then_inc(rope_turned, 1)
            mean_squares(0)

            pe.wait_ge(h_ready, KT)

            def rotate(m, j):
                pe.wait_ge(raw_ready, m + 5)
                pe.wait_ge(sin_part, m + 1)
                nc.tensor.matmul(side[j % 2][:], swap[:], raw[:, j % 2], start=True, stop=True).then_inc(rotated, 1)

            def qk_group(i):
                for j in range(SLOTS_W):
                    m = i * SLOTS_W + j
                    pe.wait_ge(raw_ready, m + 1)
                    unit(i, j, acc[j % 4], lambda c: hT[:, c], True, True)
                    if j:
                        rotate(m - 1, j - 1)
                rotate(i * SLOTS_W + SLOTS_W - 1, SLOTS_W - 1)
            with pe.Fori(0, QK // SLOTS_W) as i:
                qk_group(i)

            def v_back(j):
                pe.wait_ge(raw_ready, QK + j + 5)
                pe.wait_ge(v_ready, j + 1)
                for b in range(NB):
                    last = nc.tensor.matmul(side[2 + j % 2][:, b * P:(b + 1) * P], raw[:, j % 2, b * P:(b + 1) * P], ident[:],
                                            start=b == 0, stop=b == NB - 1)
                last.then_inc(v_turned, 1)
            for j in range(NKV):
                pe.wait_ge(raw_ready, QK + j + 1)
                unit(QK // SLOTS_W, j, acc[j % 4], lambda c: hT[:, c], True, True)
                if j:
                    v_back(j - 1)
            v_back(NKV - 1)

            with pe.Fori(0, KV2) as i:
                def parts(c):
                    return c // 8, (c // 4) % 2, c % 4

                for c in range(COMBOS + 3):
                    n = i * COMBOS + c
                    if c < COMBOS:
                        kv, hh, tile = parts(c)
                        width = (tile + 1) * P
                        if c % 8 == 0:
                            pe.wait_ge(staged, i * 2 + kv + 1)
                        pe.wait_ge(expd, n + 1)
                        pe.wait_ge(topped, n + 1)
                        nc.tensor.matmul(acc[c % 4][:, 0:width], q2[:, 2 * kv + hh, tile * P:width], k1[:, kv, 0:width],
                                         start=True, stop=False)
                        nc.tensor.matmul(acc[c % 4][:, tile * P:width], ident[:], causal[:], start=False,
                                         stop=True).then_inc(scores, 1)
                    if 0 <= c - 2 < COMBOS:
                        kv, hh, tile = parts(c - 2)
                        pe.wait_ge(normed, n - 2 + 1)
                        pe.wait_ge(probT_ready, n - 2 + 1)
                        for b in range(tile + 1):
                            last = nc.tensor.matmul(side[c % 2][:, b * P:(b + 1) * P], prob[:, (c - 2) % 4, b * P:(b + 1) * P],
                                                    ident[:], start=b == 0, stop=b == tile)
                        last.then_inc(p_turned, 1)
                    if 0 <= c - 3 < COMBOS:
                        kv, hh, tile = parts(c - 3)
                        pe.wait_ge(probT_ready, n - 3 + 1 + 2)
                        pe.wait_ge(o_ready, n - 3 + 1)
                        for b in range(tile + 1):
                            last = nc.tensor.matmul(side[2 + (c - 3) % 2][:, 0:P], v1[:, kv, b * P:(b + 1) * P],
                                                    probT[:, (c - 3) % 2, b * P:(b + 1) * P], start=b == 0, stop=b == tile)
                        last.then_inc(o_done, 1)

            pe.wait_ge(o_ready, KV2 * COMBOS + 2)
            for m in range(KT):
                if m >= 4:
                    pe.wait_ge(attn_ready, m - 3)
                for part in range(2):
                    u = U_WO + 2 * m + part
                    last = unit(u // SLOTS_W, u % SLOTS_W, acc[m % 4], lambda c: big[:, (part * KT + c) * S:(part * KT + c + 1) * S],
                                part == 0, part == 1)
            mean_squares(1)

            pe.wait_ge(h_ready, 2 * KT)
            with pe.Fori(0, NI // 4) as i:
                for j in range(4):
                    m = i * 4 + j
                    pe.wait_ge(silu_ready, m + 1)
                    unit(i + U_MLP // SLOTS_W, 2 * j, acc[j % 2], lambda c: hT[:, c], True, True)
                    pe.wait_ge(act_ready, m + 1)
                    unit(i + U_MLP // SLOTS_W, 2 * j + 1, acc[2 + j % 2], lambda c: hT[:, c], True, True)
            pe.wait_ge(act_ready, NI + 2)
            with pe.Fori(0, KT // 2) as i:
                for j in range(2):
                    pe.wait_ge(branch_ready, i * 2 + j + 1)
                    for part in range(4):
                        unit(i + U_DOWN // SLOTS_W, 4 * j + part, side[j],
                             lambda c: big[:, (part * KT + c) * S:(part * KT + c + 1) * S], part == 0, part == 3)

            pe.wait_ge(branch_ready, KT + 2)
            for b in range(NB):
                if b >= 2:
                    pe.wait_ge(rows_ready, b - 1)
                for c in range(KT):
                    last = nc.tensor.matmul(acc[2 * (b % 2) + c // 4][:, (c % 4) * P:(c % 4 + 1) * P],
                                            branch[:, c, b * P:(b + 1) * P], ident[:], start=c % 4 == 0, stop=c % 4 == 3)
                last.then_inc(back, 1)

        @block.scalar
        def _(act):
            act.sem_inc(raw_ready, 4)
            act.sem_inc(expd, 4)
            act.sem_inc(probT_ready, 2)
            act.sem_inc(o_ready, 2)
            act.sem_inc(silu_ready, 2)
            act.wait_ge(small, 64)
            nc.scalar.activation(tg[:], tg[:], ACT.Tanh).then_inc(tg_ready, 1)
            act.wait_ge(shift_ready, 1)
            for b in range(NB):
                nc.scalar.activation(hid[:, b * DI:(b + 1) * DI], rows[:, b], ACT.Identity, bias=shift[:, b:b + 1],
                                     scale=rstd[:, b:b + 1]).then_inc(hid_ready, 1)
            for c in range(KT):
                act.wait_ge(turned, c + 1)
                nc.scalar.activation(xT[:, c], acc[c % 4][:], ACT.Copy).then_inc(turned_out, 1)
                act.wait_ge(square_used, c + 1)
                nc.scalar.activation(square[:, c % 4], acc[c % 4][:], ACT.Square).then_inc(square_ready, 1)
            for r in range(2):
                act.wait_ge(rope_turned, r + 1)
                nc.scalar.activation(rope[:, r], side[2 + r][:], ACT.Copy).then_inc(rope_ready, 1)
            act.wait_ge(score_ready, NB)
            nc.scalar.activation(coef[:], score[:], ACT.Exp, scale=-1.0).then_inc(e_ready, 1)

            with act.Fori(0, QK // SLOTS_W) as i:
                for j in range(SLOTS_W):
                    m = i * SLOTS_W + j
                    act.wait_ge(w_used, SLOTS_W + m + 1)
                    act.wait_ge(rotated, m + 1)
                    act.wait_ge(cos_part, m + 1)
                    nc.scalar.activation(raw[:, j % 2], acc[j % 4][:], ACT.Identity,
                                         bias=cols[:, bass.ds(m, 1)]).then_inc(raw_ready, 1)
            for j in range(NKV):
                act.wait_ge(w_used, SLOTS_W + QK + j + 1)
                if j < 2:
                    act.wait_ge(rotated, QK + 2)
                    act.wait_ge(cos_part, QK + 2)
                else:
                    act.wait_ge(v_turned, j - 1)
                nc.scalar.activation(raw[:, j % 2], acc[j % 4][:], ACT.Identity,
                                     bias=cols[:, QK + j:QK + j + 1]).then_inc(raw_ready, 1)

            with act.Fori(0, KV2) as i:
                for c in range(COMBOS + 3):
                    n = i * COMBOS + c
                    if c < COMBOS:
                        width = (c % 4 + 1) * P
                        act.wait_ge(biased, n + 1)
                        act.wait_ge(p_turned, n + 1)
                        nc.scalar.activation(prob[:, c % 4, 0:width], acc[c % 4][:, 0:width], ACT.Exp,
                                             bias=bias[:, c % 4:c % 4 + 1], scale=SCALE,
                                             accum_out=total[:, c % 4:c % 4 + 1]).then_inc(expd, 1)
                    if 0 <= c - 2 < COMBOS:
                        width = ((c - 2) % 4 + 1) * P
                        act.wait_ge(p_turned, n - 2 + 1 + 4)
                        act.wait_ge(o_done, n - 2 - 1 + COMBOS)
                        nc.scalar.activation(probT[:, c % 2, 0:width], side[c % 2][:, 0:width], ACT.Copy).then_inc(probT_ready, 1)
                    if 0 <= c - 3 < COMBOS:
                        d = c - 3
                        act.wait_ge(o_done, n - 3 + 1 + COMBOS)
                        at = (i * 4 + d // 4) * S + (d % 4) * P
                        nc.scalar.activation(big[:, bass.ds(at, P)], side[2 + d % 2][:, 0:P], ACT.Copy).then_inc(o_ready, 1)

            act.wait_ge(base_ready, NB)
            for m in range(KT + 1):
                if m < KT:
                    act.wait_ge(w_used, SLOTS_W + U_WO + 2 * m + 2)
                    nc.scalar.activation(branch[:, m], acc[m % 4][:], ACT.Copy).then_inc(attn_ready, 1)
                if m:
                    act.wait_ge(x1_ready, m)
                    act.wait_ge(square_used, KT + m)
                    nc.scalar.activation(square[:, (m - 1) % 4], xT[:, m - 1], ACT.Square).then_inc(square_ready, 1)
            with act.Fori(0, NI // 4) as i:
                for j in range(4):
                    m = i * 4 + j
                    act.wait_ge(w_used, SLOTS_W + U_MLP + 2 * m + 1)
                    act.wait_ge(act_ready, m + 1)
                    nc.scalar.activation(silu[:, j % 2], acc[j % 2][:], ACT.Silu).then_inc(silu_ready, 1)

        @block.vector
        def _(dve):
            dve.sem_inc(cos_part, 2)
            dve.sem_inc(sin_part, 2)
            dve.sem_inc(qk_ready, 2)
            dve.sem_inc(v_ready, 2)
            dve.sem_inc(topped, 4)
            dve.sem_inc(act_ready, 2)
            dve.sem_inc(branch_ready, 2)
            chain = Chain(dve, chain_s)
            dve.wait_ge(pos_in, 16)
            nc.vector.tensor_copy(pos_i[:], pos[:]).then_inc(idx_ready, 1)
            for b in range(NB):
                chain.did(nc.vector.tensor_scalar(row_f[:, b:b + 1], pos[:, b:b + 1], float(b * L), None, ALU.add))
            chain.wait()
            nc.vector.tensor_copy(row_i[:], row_f[:]).then_inc(idx_ready, 1)

            for b in range(NB):
                dve.wait_ge(x_in[b], 16)
                for h in range(H2):
                    chain.did(nc.vector.bn_stats(stats[:, b, 6 * h:6 * h + 6], halves(rows[:, b], h)))
            for b in range(NB):
                chain.wait()
                chain.did(nc.vector.bn_aggr(mv[:, b], stats[:, b]))
            chain.wait()
            nc.vector.tensor_scalar(mv[:, :, 1], mv[:, :, 1], LN_EPS, None, ALU.add).then_inc(var_ready, 1)
            dve.wait_ge(rstd_ready, 1)
            nc.vector.scalar_tensor_tensor(out=shift[:], in0=mv[:, :, 0], scalar=-1.0, in1=rstd[:],
                                           op0=ALU.mult, op1=ALU.mult).then_inc(shift_ready, 1)
            dve.wait_ge(small, 64)
            dve.wait_ge(tg_ready, 1)
            scrap = work[:, 12:14].rearrange("p a s -> p (a s)")
            for b in range(NB):
                dve.wait_ge(hid_ready, b + 1)
                if b:
                    dve.wait_ge(score_ready, b)
                nc.vector.tensor_tensor_reduce(out=scrap, in0=hid[:, b * DI:(b + 1) * DI], in1=router[:], scale=1.0, scalar=0.0,
                                               op0=ALU.mult, op1=ALU.add, accum_out=score[:, b:b + 1]).then_inc(score_ready, 1)
                nc.vector.scalar_tensor_tensor(out=rows[:, b], in0=hid[:, b * DI:(b + 1) * DI], scalar=tg[:, 1:2], in1=rows[:, b],
                                               op0=ALU.mult, op1=ALU.add).then_inc(base_ready, 1)

            def norm(r):
                dve.wait_ge(square_used, 4 + KT * (r + 1))
                nc.vector.tensor_scalar(rms[:], side[0][:], 1.0 / DI, RMS_EPS, ALU.mult, ALU.add).then_inc(mean_ready, 1)
                dve.wait_ge(pow_ready, r + 1)
                if r == 0:
                    dve.wait_ge(turned_out, KT)
                for c in range(KT):
                    ln = QK + NKV + r * KT + c
                    nc.vector.scalar_tensor_tensor(out=hT[:, c], in0=xT[:, c], scalar=cols[:, ln:ln + 1], in1=rms[:],
                                                   op0=ALU.mult, op1=ALU.mult).then_inc(h_ready, 1)
            norm(0)
            dve.wait_ge(e_ready, 1)
            chain.did(nc.vector.tensor_scalar(coef[:], coef[:], 1.0, None, ALU.add))
            chain.wait()
            chain.did(nc.vector.reciprocal(coef[:], coef[:]))
            chain.wait()
            nc.vector.tensor_scalar(coef[:], coef[:], tg[:, 1:2], None, ALU.mult).then_inc(coef_ready, 1)

            dve.wait_ge(rope_ready, 2)
            with dve.Fori(0, QK // SLOTS_W) as i:
                for j in range(SLOTS_W):
                    m = i * SLOTS_W + j
                    dve.wait_ge(raw_ready, m + 5)
                    dve.wait_ge(qk_ready, m + 1)
                    nc.vector.tensor_tensor(part_c[:, j % 2], raw[:, j % 2], rope[:, 0], ALU.mult).then_inc(cos_part, 1)
                    dve.wait_ge(rotated, m + 3)
                    nc.vector.tensor_tensor(part_s[:, j % 2], side[j % 2][:], rope[:, 1], ALU.mult).then_inc(sin_part, 1)
                    dve.wait_ge(sin_part, m + 3)
                    nc.vector.tensor_tensor(big[:, bass.ds(m * S, S)], part_c[:, j % 2], part_s[:, j % 2],
                                            ALU.add).then_inc(qk_ready, 1)
            for j in range(NKV):
                dve.wait_ge(v_turned, j + 1)
                nc.vector.tensor_copy(v[:, j * S:(j + 1) * S], side[2 + j % 2][:]).then_inc(v_ready, 1)
            dve.wait_ge(qk_ready, QK + 2)
            dve.wait_ge(v_ready, NKV + 2)

            def stage(i, kv):
                dve.wait_ge(o_done, i * COMBOS + 8 * kv + 8)
                for hh in range(2):
                    nc.vector.tensor_copy(q2[:, 2 * kv + hh], big[:, bass.ds((i * 4 + kv * 2 + hh) * S, S)])
                nc.vector.tensor_copy(k1[:, kv], big[:, bass.ds((i * 2 + kv + NH) * S, S)])
                nc.vector.tensor_copy(v1[:, kv], big[:, bass.ds((i * 2 + kv + QK) * S, S)]).then_inc(staged, 1)

            with dve.Fori(0, KV2) as i:
                for c in range(COMBOS + 1):
                    n = i * COMBOS + c
                    if c in (0, 4):
                        stage(i, c // 4)
                    if c < COMBOS:
                        one = slice(c % 4, c % 4 + 1)
                        dve.wait_ge(scores, n + 1)
                        nc.vector.tensor_reduce(top[:, one], acc[c % 4][:, 0:(c % 4 + 1) * P], AXX, ALU.max).then_inc(topped, 1)
                        dve.wait_ge(topped, n + 5)
                        dve.wait_ge(expd, n + 1)
                        nc.vector.tensor_scalar(bias[:, one], top[:, one], -SCALE, None, ALU.mult).then_inc(biased, 1)
                    if c >= 1:
                        d = (c - 1) % 4
                        dve.wait_ge(expd, n - 1 + 1 + 4)
                        nc.vector.reciprocal(inv[:, d:d + 1], total[:, d:d + 1]).then_inc(inverted, 1)
                        dve.wait_ge(inverted, n)
                        nc.vector.tensor_scalar(prob[:, d, 0:(d + 1) * P], prob[:, d, 0:(d + 1) * P], inv[:, d:d + 1], None,
                                                ALU.mult).then_inc(normed, 1)

            for m in range(KT):
                dve.wait_ge(attn_ready, m + 1)
                nc.vector.tensor_tensor(xT[:, m], xT[:, m], branch[:, m], ALU.add).then_inc(x1_ready, 1)
            norm(1)
            with dve.Fori(0, NI // 4) as i:
                for j in range(4):
                    m = i * 4 + j
                    dve.wait_ge(silu_ready, m + 3)
                    dve.wait_ge(w_used, SLOTS_W + U_MLP + 2 * m + 2)
                    nc.vector.tensor_tensor(big[:, bass.ds(m * S, S)], silu[:, j % 2], acc[2 + j % 2][:], ALU.mult).then_inc(act_ready, 1)
            with dve.Fori(0, KT // 2) as i:
                for j in range(2):
                    m = i * 2 + j
                    dve.wait_ge(w_used, SLOTS_W + U_DOWN + 4 * m + 4)
                    nc.vector.tensor_tensor(hid[:, bass.ds(m * S, S)], hid[:, bass.ds(m * S, S)], side[j][:],
                                            ALU.add).then_inc(branch_ready, 1)
            dve.wait_ge(coef_ready, 1)
            dve.wait_ge(base_ready, NB)
            for b in range(NB):
                dve.wait_ge(back, b + 1)
                for h in range(H2):
                    last = nc.vector.scalar_tensor_tensor(out=halves(rows[:, b], h), in0=acc[2 * (b % 2) + h][:],
                                                          scalar=coef[:, b:b + 1], in1=halves(rows[:, b], h),
                                                          op0=ALU.mult, op1=ALU.add)
                last.then_inc(rows_ready, 1)

SCRATCH = dict(ug=(STEPS * P, 2 * L), xd=(NB * ND, L), x2=(NB * L, DI), pos=(P, NB))
SCRATCH_KIND = "Internal"
STAGES = (project_stage, scan_stage, route_stage, layer_stage)


def build(nc, t):
    for stage in STAGES:
        with nc.cleanup_on_exit(), ExitStack() as ctx:
            stage(nc, t, ctx)


def kernel(x, ctx_1024, g_xattn, g_ffn, L0_xattn_in_proj_w, L0_xattn_conv_w, L0_xattn_conv_b, L0_xattn_x_proj_w,
           L0_xattn_dt_proj_w, L0_xattn_dt_proj_b, L0_xattn_A_log, L0_xattn_D, L0_ffn_w_router, L0_ffn_wq, L0_ffn_bq,
           L0_ffn_wk, L0_ffn_bk, L0_ffn_wv, L0_ffn_bv, L0_ffn_wo, L0_ffn_w_gate, L0_ffn_w_up, L0_ffn_w_down,
           L0_ffn_ln1_w, L0_ffn_ln2_w):
    import concourse.bacc as _bacc
    from concourse.bass_utils import run_bass_kernel_spmd as _run

    def flat(a):
        return np.ascontiguousarray(a)

    def tiles(w):
        w = np.asarray(w)
        return flat(w.reshape(w.shape[0] // P, P, w.shape[1] // P, P).transpose(2, 1, 0, 3)).reshape(w.shape[1], w.shape[0])

    def column(v):
        return flat(np.asarray(v).reshape(-1, P).T)

    def conv_params(w, bias):
        return flat(np.concatenate([np.asarray(w), np.asarray(bias)[:, None]], 1).reshape(NE, P, TAPS + 1).transpose(1, 0, 2))

    inv_freq = (np.float32(1.0) / np.float32(10000.0) ** (np.arange(0, DH, 2, dtype=np.float32) / np.float32(DH))).astype(np.float32)
    angle = np.arange(L, dtype=np.float32)[:, None] * inv_freq
    rope = np.concatenate([np.cos(angle), np.cos(angle), np.sin(angle), np.sin(angle)], 1).astype(np.float32)
    counts = np.concatenate([np.tile(np.arange(P), (P, 1)), np.arange(P)[:, None] + P * np.arange(L // P)], 1).astype(np.float32)
    swap = np.zeros((P, P), np.float32)
    swap[np.arange(64) + 64, np.arange(64)] = -1.0
    swap[np.arange(64), np.arange(64) + 64] = 1.0
    arrays = dict(
        x=flat(x).reshape(NB * L, DI),
        ctxT=flat(np.asarray(ctx_1024).reshape(NB, L, NK, P).transpose(0, 3, 2, 1)).reshape(NB, P, NK * L),
        g=flat(np.concatenate([np.asarray(g_xattn), np.asarray(g_ffn)])).reshape(1, 2),
        w_in=flat(np.asarray(L0_xattn_in_proj_w).T.reshape(NK, P, DI).transpose(1, 0, 2)),
        w_x=flat(np.asarray(L0_xattn_x_proj_w).T.reshape(NE, P, ND).transpose(1, 0, 2)),
        conv=conv_params(L0_xattn_conv_w, L0_xattn_conv_b),
        w_dt=flat(np.asarray(L0_xattn_dt_proj_w).reshape(NE, P, NR).transpose(0, 2, 1)).reshape(NE * NR, P),
        ssm=flat(np.concatenate([np.asarray(L0_xattn_A_log), np.asarray(L0_xattn_dt_proj_b)[:, None],
                                 np.asarray(L0_xattn_D)[:, None]], 1)),
        router=flat(L0_ffn_w_router).reshape(1, DI),
        wq=tiles(L0_ffn_wq), wk=tiles(L0_ffn_wk), wv=tiles(L0_ffn_wv), wo=tiles(L0_ffn_wo),
        w_gate=tiles(L0_ffn_w_gate), w_up=tiles(L0_ffn_w_up), w_down=tiles(L0_ffn_w_down),
        cols=flat(np.concatenate([column(L0_ffn_bq), column(L0_ffn_bk), column(L0_ffn_bv), column(L0_ffn_ln1_w),
                                  column(L0_ffn_ln2_w)], 1)),
        rope=rope, swap=swap, counts=counts,
    )
    nc = _bacc.Bacc("TRN2", target_bir_lowering=False, num_devices=1)
    t, named = {}, {}
    for name, a in arrays.items():
        named[f"in_{name}"] = a
        t[name] = nc.dram_tensor(f"in_{name}", a.shape, mybir.dt.from_np(a.dtype), kind="ExternalInput").ap()
    for name, shape in SCRATCH.items():
        t[name] = nc.dram_tensor(f"scratch_{name}", shape, F32, kind=SCRATCH_KIND).ap()
    t["out"] = nc.dram_tensor("out_0_dram", (NB * L, DI), F32, kind="ExternalOutput").ap()
    build(nc, t)
    r = _run(nc, [named], core_ids=[0])
    return r.results[0]["out_0_dram"].reshape(NB, L, DI)
```
